# Optimizing a Trainium2 kernel written in Bass

```python
import numpy as np
import jax
import jax.numpy as jnp

def _softmax(x, axis=-1):
    return jax.nn.softmax(x, axis=axis)

def _gelu(x):
    return jax.nn.gelu(x, approximate=True)

def _silu(x):
    return jax.nn.silu(x)

def _sigmoid(x):
    return jax.nn.sigmoid(x)

def _layernorm(x, axis=-1, eps=1e-05):
    m = jnp.mean(x, axis=axis, keepdims=True)
    v = jnp.var(x, axis=axis, keepdims=True)
    return (x - m) / jnp.sqrt(v + eps)

def _scatter_add(tgt, idx, src, axis=0):
    return tgt.at[idx].add(src)

def _segment_sum(src, seg, n):
    return jax.ops.segment_sum(src, seg, n)
kernel_name = 'mk_cond_resid_d2_seqx_r4_3ade89'

def setup_inputs(seed: int=0):
    np.random.seed(seed)
    _w = jnp.asarray

    def _rec_inputs():
        import jax
        import jax.numpy as jnp
        _rk = jax.random.key(seed)
        x = -0.000125 + 0.9999 * jax.random.normal(jax.random.fold_in(_rk, 1), (128, 64, 1024), jnp.float32)
        _lenS = 64 - jax.random.randint(jax.random.fold_in(_rk, 7), (128,), 0, max(1, 64 // 4) + 1, jnp.int32)
        _lenS2 = 64 - jax.random.randint(jax.random.fold_in(_rk, 8), (128,), 0, max(1, 64 // 4) + 1, jnp.int32)
        cond_128 = 0.0061147 + 1.02565 * jax.random.normal(jax.random.fold_in(_rk, 11), (128, 128), jnp.float32)
        fside_S_0 = -0.022604 + 0.987366 * jax.random.normal(jax.random.fold_in(_rk, 12), (64,), jnp.float32)
        return (x, cond_128, fside_S_0)
    x, cond_128, fside_S_0 = _rec_inputs()

    def _L0_cond_setup():
        import jax, jax.numpy as jnp
        import numpy as np
        from jax import lax
        N, C_IN, L = (32, 64, 1024)
        C_OUT, K, GROUPS = (64, 9, 4)
        C_DIM, PAD, STRIDE = (128, 4, 1)
        key = jax.random.key(seed)
        k1, k2, k3, k4, k5 = jax.random.split(key, 5)
        x = jax.random.normal(k1, (N, C_IN, L), dtype=jnp.float32)
        c = jax.random.normal(k2, (N, C_DIM), dtype=jnp.float32)
        weight = jax.random.normal(k3, (C_OUT, C_IN // GROUPS, K), dtype=jnp.float32)
        c_weight = jax.random.normal(k4, (C_OUT, C_DIM), dtype=jnp.float32)
        bias = jax.random.normal(k5, (C_OUT,), dtype=jnp.float32)
        return {'x': x, 'c': c, 'weight': weight, 'c_weight': c_weight, 'bias': bias}
    _L0_cond_all = _L0_cond_setup()
    _L0_cond_in = {k: v for k, v in _L0_cond_all.items() if k in ('weight', 'c_weight')}
    del _L0_cond_all

    def _L1_cond_setup():
        import jax, jax.numpy as jnp
        import numpy as np
        K = 8
        T = 1.0
        D_EMBD = 128
        IN_C = 64
        OUT_C = 64
        BS = 32
        H = 1024
        HID = 128
        key = jax.random.key(seed)
        ks = jax.random.split(key, 10)
        s = lambda fan_in: 1.0 / np.sqrt(fan_in)
        return {'x': jax.random.normal(ks[0], (BS, IN_C, H), dtype=jnp.float32), 'embedding': jax.random.normal(ks[1], (BS, D_EMBD), dtype=jnp.float32), 'W0': jax.random.normal(ks[2], (D_EMBD, HID), dtype=jnp.float32) * s(D_EMBD), 'b0': jnp.zeros((HID,), dtype=jnp.float32), 'W1': jax.random.normal(ks[3], (HID, HID), dtype=jnp.float32) * s(HID), 'b1': jnp.zeros((HID,), dtype=jnp.float32), 'W2': jax.random.normal(ks[4], (HID, K), dtype=jnp.float32) * s(HID), 'b2': jnp.zeros((K,), dtype=jnp.float32), 'weight': jax.random.normal(ks[5], (K, OUT_C, IN_C, 1), dtype=jnp.float32) * s(IN_C), 'bias_k': jax.random.normal(ks[6], (K, OUT_C), dtype=jnp.float32) * 0.1}
    _L1_cond_all = _L1_cond_setup()
    _L1_cond_in = {k: v for k, v in _L1_cond_all.items() if k in ('W0', 'b0', 'W1', 'b1', 'W2', 'b2', 'weight', 'bias_k')}
    del _L1_cond_all
    return {'x': x, 'cond_128': cond_128, 'fside_S_0': fside_S_0, 'L0_cond_weight': _L0_cond_in['weight'], 'L0_cond_c_weight': _L0_cond_in['c_weight'], 'L1_cond_W0': _L1_cond_in['W0'], 'L1_cond_b0': _L1_cond_in['b0'], 'L1_cond_W1': _L1_cond_in['W1'], 'L1_cond_b1': _L1_cond_in['b1'], 'L1_cond_W2': _L1_cond_in['W2'], 'L1_cond_b2': _L1_cond_in['b2'], 'L1_cond_weight': _L1_cond_in['weight'], 'L1_cond_bias_k': _L1_cond_in['bias_k']}

def reference(x, cond_128, fside_S_0, L0_cond_weight, L0_cond_c_weight, L1_cond_W0, L1_cond_b0, L1_cond_W1, L1_cond_b1, L1_cond_W2, L1_cond_b2, L1_cond_weight, L1_cond_bias_k):
    import jax
    import jax.numpy as jnp

    def _L0_cond_ref(x, c, weight, c_weight, bias):
        import jax, jax.numpy as jnp
        import numpy as np
        from jax import lax
        N, C_IN, L = (32, 64, 1024)
        C_OUT, K, GROUPS = (64, 9, 4)
        C_DIM, PAD, STRIDE = (128, 4, 1)
        out = lax.conv_general_dilated(x, weight, window_strides=(STRIDE,), padding=[(PAD, PAD)], dimension_numbers=('NCH', 'OIH', 'NCH'), feature_group_count=GROUPS)
        ctx = jnp.einsum('nd,od->no', c, c_weight)
        out = out + ctx[:, :, None] + bias[None, :, None]
        return out

    def _L1_cond_ref(x, embedding, W0, b0, W1, b1, W2, b2, weight, bias_k):
        import jax, jax.numpy as jnp
        import numpy as np
        K = 8
        T = 1.0
        D_EMBD = 128
        IN_C = 64
        OUT_C = 64
        BS = 32
        H = 1024
        HID = 128
        h = jax.nn.gelu(embedding @ W0 + b0, approximate=False)
        h = jax.nn.gelu(h @ W1 + b1, approximate=False)
        att = jax.nn.softmax((h @ W2 + b2) / T, axis=-1)
        agg_w = jnp.einsum('bk,koi->boi', att, weight[..., 0])
        agg_b = att @ bias_k
        out = jnp.einsum('boi,bih->boh', agg_w, x) + agg_b[:, :, None]
        return out
    x = x + _L0_cond_ref(x, cond_128, L0_cond_weight, L0_cond_c_weight, fside_S_0)
    x = x + _L1_cond_ref(x, cond_128, L1_cond_W0, L1_cond_b0, L1_cond_W1, L1_cond_b1, L1_cond_W2, L1_cond_b2, L1_cond_weight, L1_cond_bias_k)
    return x

_drawn_inputs = setup_inputs


def setup_inputs(seed=0):
    import zlib

    import numpy as np

    out = dict(_drawn_inputs(seed))
    spreads = {'L1_cond_b0': (0.0, 0.607), 'L1_cond_b1': (0.0, 0.431), 'L1_cond_b2': (0.0, 0.337)}
    factors = {'L1_cond_bias_k': 28.039}
    for name, (base, spread) in spreads.items():
        noise = np.random.default_rng([zlib.crc32(name.encode()), seed]).standard_normal(out[name].shape)
        drawn = base * np.exp(spread * noise) if base else spread * noise
        out[name] = jnp.asarray(drawn.astype(out[name].dtype))
    for name, factor in factors.items():
        out[name] = (out[name] * factor).astype(out[name].dtype)
    return out
```

```python
from contextlib import ExitStack

import numpy as np

import concourse.bass as bass
from concourse import mybir

F32 = mybir.dt.float32
F32R = mybir.dt.float32r
I32 = mybir.dt.int32
ALU = mybir.AluOpType
ACT = mybir.ActivationFunctionType
AX = mybir.AxisListType

P = 128
NS, C, L = 128, 64, 1024
G, TAPS, PAD = 4, 9, 4
CG = C // G
KQ = 4
PH = 8
NJ = L // PH
JB = NJ // 32
CC = CG // KQ
SG = 2 * G
S = 4
NB = NS // S
PR = S // 2
NP = NS // 2
KE = 8
D = 128
XW = PAD + PR * L
TJ = NJ + 1
BANK = 512


def build(nc, x, cond_t, cw_t, fside, conv_w, w0, b0, w1, b1, w2, b2, mix_w, bias_k, consts, edge_bits, out):
    ctx = ExitStack()
    with ctx:
        def sb(name, shape, dt=F32):
            return ctx.enter_context(nc.sbuf_tensor(name, shape, dt))

        def ps(name, shape):
            return ctx.enter_context(nc.psum_tensor(name, shape, F32))

        def sem(name):
            return ctx.enter_context(nc.semaphore(name))

        xin = [sb(f"xin{i}", [P, XW]) for i in range(2)]
        xcol = sb("xcol", [P, PR * JB, PH, CC * SG])
        xph = [sb(f"xph{i}", [P, S, G, TJ]) for i in range(2)]
        xhi = [sb(f"xhi{i}", [P, S, G, TJ], F32R) for i in range(2)]
        xlo = [sb(f"xlo{i}", [P, S, G, TJ], F32R) for i in range(2)]
        ycol = sb("ycol", [P, PR * JB, PH * CC, 2, G])
        yz = sb("yz", [P, 4, PR, L])
        ynat = [yz[:, i] for i in range(2)]
        zout = [yz[:, 2 + i] for i in range(2)]
        mixw = yz[0:KE].rearrange("e a r l -> e (a r l)").rearrange("e (o p) -> e o p", p=P)
        mixt = sb("mixt", [P, CG, G, NS])
        mixv = [sb(f"mixv{i}", [P, PR, P]) for i in range(2)]
        wraw = sb("wraw", [P, 2, G, P])
        whi = sb("whi", [P, 2, G, P], F32R)
        wlo = sb("wlo", [P, 2, G, P], F32R)
        CW = 2 * P + P + C + 2
        cst = sb("cst", [P, CW])
        condt = sb("condt", [P, NS])
        cwt = sb("cwt", [P, P])
        w0s, w1s, w2s = sb("w0s", [P, D]), sb("w1s", [P, D]), sb("w2s", [P, KE])
        cols = sb("cols", [P, 3])
        b2s = sb("b2s", [1, KE])
        bks = sb("bks", [KE, P])
        ones = sb("ones", [1, P])
        ebits = sb("ebits", [P, 2], I32)
        h1, h2 = sb("h1", [P, NS]), sb("h2", [P, NS])
        negmax, esum, erec = sb("negmax", [P, 1]), sb("esum", [P, 1]), sb("erec", [P, 1])
        expv, att, attt = sb("expv", [P, KE]), sb("att", [P, KE]), sb("attt", [KE, NS])
        full = sb("full", [P, 2, NS])
        half = sb("half", [P, 2, NP])
        beta = sb("beta", [P, 2, NP])
        gam = [sb(f"gam{i}", [P, PR]) for i in range(2)]
        at = 0
        residual = cst[:, at:at + 2 * P].rearrange("p (b c) -> p b c", b=2); at += 2 * P
        ident = cst[:, at:at + P]; at += P
        same = cst[:, at:at + C]; at += C
        smask = cst[:, at:at + 2];

        yps = [ps(f"yps{g}", [P, 2, PR * NJ]) for g in range(G)]
        zps = ps("zps", [P, L])
        gps = ps("gps", [P, BANK])
        sps = ps("sps", [P, BANK])

        x_in = [sem(f"x_in{i}") for i in range(2)]
        z_out = [sem(f"z_out{i}") for i in range(2)]
        p_in, pm_in, pw_in = sem("p_in"), sem("pm_in"), sem("pw_in")
        wrapped = sem("wrapped")
        cols_made = sem("cols_made")
        turned = sem("turned")
        edged = sem("edged")
        hi_made = sem("hi_made")
        lo_made = sem("lo_made")
        conv_done = sem("conv_done")
        ycol_made = sem("ycol_made")
        ynat_made = sem("ynat_made")
        mixv_made = sem("mixv_made")
        gam_mm = sem("gam_mm")
        gam_made = sem("gam_made")
        mix_done = sem("mix_done")
        z_made = sem("z_made")
        zeroed = sem("zeroed")
        w_sum, w_hi, w_lo = sem("w_sum"), sem("w_hi"), sem("w_lo")
        mm, gelu, sm, b_act, b_dve, agg_mm, agg_out = (sem(n) for n in (
            "mm", "gelu", "sm", "b_act", "b_dve", "agg_mm", "agg_out"))

        def x_rows(t, pair):
            return t.rearrange("(n s) (g c) l -> n c (s g) l", s=2, g=G)[bass.ds(pair, 1)].rearrange(
                "n c q l -> (n c) q l")

        block = ctx.enter_context(nc.Block())

        @block.sync
        def _(sp):
            def load(n, slot):
                if not (isinstance(n, int) and n < 2):
                    sp.wait_ge(cols_made, n - 1)
                for r in range(PR):
                    sp.dma_start(xin[slot][:, PAD + r * L:PAD + r * L + L], x_rows(x, 2 * n + r)).then_inc(x_in[slot], 16)

            def store(n, slot):
                for r in range(PR):
                    sp.wait_ge(z_made, 2 * n + r + 1)
                    sp.dma_start(x_rows(out, 2 * n + r), zout[slot][:, r]).then_inc(z_out[slot], 16)

            sp.dma_start(wraw[:], conv_w).then_inc(pw_in, 16)
            sp.dma_start(cst[:], consts).then_inc(pw_in, 16)
            sp.dma_start(ebits[:], edge_bits).then_inc(pw_in, 16)
            load(0, 0)
            load(1, 1)
            load(2, 0)
            load(3, 1)
            with sp.Fori(0, NB // 2 - 2) as i:
                for c in range(2):
                    load(2 * i + c + 4, c)
                    store(2 * i + c, c)
            for n in range(NB - 4, NB):
                store(n, n % 2)
            for slot in range(2):
                sp.wait_ge(z_out[slot], 32 * (NB // 2))

        @block.gpsimd
        def _(pool):
            nc.gpsimd.memset(ones[:], 1.0).then_inc(zeroed, 1)
            pool.wait_ge(w_hi, 1)
            nc.gpsimd.tensor_tensor(wlo[:], wraw[:], whi[:].bitcast(F32), ALU.subtract).then_inc(w_lo, 1)

            def low(n, slot):
                for h in range(2):
                    pool.wait_ge(hi_made, 2 * n + h + 1)
                    g = slice(2 * h, 2 * h + 2)
                    nc.gpsimd.tensor_tensor(xlo[slot][:, :, g], xph[slot][:, :, g], xhi[slot][:, :, g].bitcast(F32),
                                            ALU.subtract).then_inc(lo_made, 1)

            def matrices(n, slot):
                if not (isinstance(n, int) and n < 2):
                    pool.wait_ge(mix_done, 2 * n - 2)
                for r in range(PR):
                    nc.gpsimd.tensor_tensor(
                        mixv[slot][:, r].rearrange("p (c s g) -> p c s g", c=CG, s=2),
                        mixt[:, :, :, bass.ds(4 * n + 2 * r, 2)].rearrange("p c g s -> p c s g"),
                        smask.unsqueeze(1).unsqueeze(3).broadcast_to([P, CG, 2, G]),
                        ALU.mult).then_inc(mixv_made, 1)

            low(0, 0)
            low(1, 1)
            pool.wait_ge(agg_out, C // 4)
            matrices(0, 0)
            low(2, 0)
            matrices(1, 1)
            low(3, 1)
            matrices(2, 0)
            low(4, 0)
            with pool.Fori(1, NB // 2 - 2) as i:
                for c in range(2):
                    matrices(2 * i + c + 1, 1 - c)
                    low(2 * i + c + 3, 1 - c)
            matrices(NB - 3, 1)
            low(NB - 1, 1)
            matrices(NB - 2, 0)
            matrices(NB - 1, 1)

        @block.scalar
        def _(act):
            for k, (dst, src) in enumerate((
                    (condt, cond_t), (w0s, w0), (w1s, w1), (w2s, w2), (cwt, cw_t))):
                act.dma_start(dst[:], src).then_inc(p_in, 16)
            for k, src in enumerate((b0, b1, fside)):
                act.dma_start(cols[:, k:k + 1], src).then_inc(p_in, 16)
            act.dma_start(b2s[:], b2).then_inc(p_in, 16)
            act.dma_start(bks[:], bias_k).then_inc(pm_in, 16)
            act.dma_start(mixw, mix_w).then_inc(pm_in, 16)

            def wrap(n, slot):
                act.wait_ge(x_in[slot], 32 * (n // 2 + 1) if isinstance(n, int) else 16 * n + 32 - 16 * slot)
                nc.scalar.activation(xin[slot][:, 0:PAD], xin[slot][:, PR * L:], ACT.Copy).then_inc(wrapped, 1)

            def high(n, slot):
                act.wait_ge(edged, 3 * n + 3)
                for h in range(2):
                    if not (isinstance(n, int) and n < 2):
                        act.wait_ge(conv_done, 4 * n - 6 + 2 * h)
                    g = slice(2 * h, 2 * h + 2)
                    nc.scalar.activation(xhi[slot][:, :, g], xph[slot][:, :, g], ACT.Copy).then_inc(hi_made, 1)

            def evacuate(n, slot):
                for r in range(PR):
                    act.wait_ge(gam_mm, 2 * n + r + 1)
                    nc.scalar.activation(gam[slot][:, r:r + 1], gps[:, 2 * slot + r:2 * slot + r + 1], ACT.Identity,
                                         bias=beta[:, 1, bass.ds(2 * n + r, 1)]).then_inc(gam_made, 1)
                    act.wait_ge(gam_made, 2 * n + r + 1)
                    act.wait_ge(mix_done, 2 * n + r + 1)
                    if r == 0 and not (isinstance(n, int) and n < 2):
                        act.wait_ge(z_out[slot], 32 * (n // 2) if isinstance(n, int) else 16 * n - 16 * slot)
                    nc.scalar.activation(
                        zout[slot][:, r].rearrange("p (b j q) -> p b q j", b=JB, q=PH),
                        zps[:].rearrange("p (b q j) -> p b q j", b=JB, q=PH), ACT.Identity,
                        bias=gam[slot][:, r:r + 1]).then_inc(z_made, 1)

            def around(n, slot):
                wrap(n + 4, slot)
                evacuate(n, slot)
                high(n + 3, 1 - slot)

            act.wait_ge(w_sum, 1)
            nc.scalar.activation(whi[:], wraw[:], ACT.Copy).then_inc(w_hi, 1)
            wrap(0, 0)
            wrap(1, 1)
            act.wait_ge(p_in, 16 * 9)
            act.wait_ge(mm, 1)
            nc.scalar.activation(h1[:], sps[:, 0:NS], ACT.Gelu, bias=cols[:, 0:1]).then_inc(gelu, 1)
            act.wait_ge(mm, 2)
            nc.scalar.activation(h2[:], sps[:, NS:2 * NS], ACT.Gelu, bias=cols[:, 1:2]).then_inc(gelu, 1)
            act.wait_ge(sm, 1)
            nc.scalar.activation(expv[:], sps[:, 2 * NS:2 * NS + KE], ACT.Exp, bias=negmax[:],
                                 accum_out=esum[:]).then_inc(gelu, 1)
            act.wait_ge(mm, 4)
            nc.scalar.activation(attt[:], sps[0:KE, 3 * NS:4 * NS], ACT.Copy).then_inc(gelu, 1)
            nc.scalar.activation(full[:, 0], gps[:, 0:NS], ACT.Identity, bias=cols[:, 2:3]).then_inc(b_act, 1)
            act.wait_ge(mm, 5)
            nc.scalar.activation(full[:, 1], gps[:, NS:2 * NS], ACT.Copy).then_inc(b_act, 1)
            high(0, 0)
            high(1, 1)
            wrap(2, 0)
            high(2, 0)
            wrap(3, 1)
            act.wait_ge(b_dve, 4)
            for n in range(2):
                around(n, n)
            with act.Fori(1, NB // 2 - 2) as i:
                for c in range(2):
                    around(2 * i + c, c)
            evacuate(NB - 4, 0)
            high(NB - 1, 1)
            for n in range(NB - 3, NB):
                evacuate(n, n % 2)

        @block.vector
        def _(dve):
            def columns(n, slot):
                dve.wait_ge(wrapped, n + 1)
                if not (isinstance(n, int) and n < 1):
                    dve.wait_ge(turned, 2 * n)
                nc.vector.transpose(
                    xcol[:].rearrange("q b p c -> q (b p c)"),
                    xin[slot][:, 0:PR * L].rearrange("q (b j p) -> q b p j", j=32, p=PH)).then_inc(cols_made, 1)

            def phases(n, slot, r):
                if r == 0:
                    dve.wait_ge(cols_made, n + 1)
                    if not (isinstance(n, int) and n < 2):
                        dve.wait_ge(lo_made, 2 * n - 2)
                nc.vector.transpose(
                    xph[slot][:, 2 * r:2 * r + 2, :, 0:NJ].rearrange("q s g (b j) -> q b (s g) j", j=32),
                    xcol[:, JB * r:JB * r + JB].rearrange("q b p (c h) -> q b h (p c)", c=CC)).then_inc(turned, 1)

            def edges(n, slot):
                v = xph[slot][:].bitcast(I32).rearrange("q (r s) g j -> q r (s g) j", r=PR)
                dve.wait_ge(turned, 2 * n + 2)
                for r in range(PR):
                    nc.vector.tensor_scalar(v[:, r, :, NJ], v[:, (r + 1) % PR, :, 0], ebits[:, 0:1], None,
                                            ALU.bitwise_and).then_inc(edged, 1)
                dve.wait_ge(edged, 3 * n + 2)
                nc.vector.tensor_scalar(v[:, :, :, 0], v[:, :, :, 0], ebits[:, 1:2], None,
                                        ALU.bitwise_and).then_inc(edged, 1)

            def y_columns(n, g):
                dve.wait_ge(conv_done, 4 * n + g + 1)
                if g == 0 and not (isinstance(n, int) and n < 1):
                    dve.wait_ge(ynat_made, n)
                nc.vector.transpose(ycol[:, :, :, :, g].rearrange("q b c s -> q s b c"),
                                    yps[g][:].rearrange("q s (b j) -> q s b j", j=32)).then_inc(ycol_made, 1)

            def y_natural(n, slot):
                dve.wait_ge(ycol_made, 4 * n + 4)
                if not (isinstance(n, int) and n < 2):
                    dve.wait_ge(mix_done, 2 * n - 2)
                nc.vector.transpose(ynat[slot].rearrange("q r c -> q (r c)"),
                                    ycol[:].rearrange("q b c s g -> q (b c s g)")).then_inc(ynat_made, 1)

            def ahead(n, slot):
                columns(n, slot)
                phases(n, slot, 0)
                phases(n, slot, 1)
                edges(n, slot)

            dve.wait_ge(pw_in, 48)
            nc.vector.tensor_tensor(wraw[:], wraw[:], residual.unsqueeze(2).broadcast_to([P, 2, G, P]),
                                    ALU.add).then_inc(w_sum, 1)
            ahead(0, 0)
            dve.wait_ge(mm, 3)
            nc.vector.tensor_reduce(negmax[:], sps[:, 2 * NS:2 * NS + KE], AX.X, ALU.max, negate=True).then_inc(sm, 1)
            dve.wait_ge(gelu, 3)
            nc.vector.reciprocal(erec[:], esum[:]).then_inc(sm, 1)
            dve.wait_ge(sm, 2)
            nc.vector.tensor_scalar(att[:], expv[:], erec[:], None, ALU.mult).then_inc(sm, 1)
            dve.wait_ge(b_act, 2)
            for k in range(2):
                nc.vector.tensor_scalar(half[:, k], full[:, k, 0::2], smask[:, 0:1], None, ALU.mult).then_inc(b_dve, 1)
            for k in range(2):
                dve.wait_ge(b_dve, 1 + k)
                nc.vector.scalar_tensor_tensor(out=beta[:, k], in0=full[:, k, 1::2], scalar=smask[:, 1:2],
                                               in1=half[:, k], op0=ALU.mult, op1=ALU.add).then_inc(b_dve, 1)
            for a in range(C // 4):
                dve.wait_ge(agg_mm, a + 1)
                nc.vector.tensor_tensor(
                    mixt[:].rearrange("p c g b -> p (c g) b")[:, 4 * a:4 * a + 4], 
                    yps[a % G][:].rearrange("p s (o b) -> p (s o) b", b=NS),
                    same[:, 4 * a:4 * a + 4].unsqueeze(2).broadcast_to([P, 4, NS]), ALU.add).then_inc(agg_out, 1)
            ahead(1, 1)
            ahead(2, 0)

            def step(n, slot, more=True):
                y_columns(n, 0)
                if more:
                    columns(n + 3, 1 - slot)
                y_columns(n, 1)
                if more:
                    phases(n + 3, 1 - slot, 0)
                y_columns(n, 2)
                if more:
                    phases(n + 3, 1 - slot, 1)
                y_columns(n, 3)
                if more:
                    edges(n + 3, 1 - slot)
                y_natural(n, slot)

            for n in range(2):
                step(n, n)
            with dve.Fori(1, NB // 2 - 2) as i:
                for c in range(2):
                    step(2 * i + c, c)
            step(NB - 4, 0)
            for n in range(NB - 3, NB):
                step(n, n % 2, more=False)

        @block.tensor
        def _(pe):
            pe.wait_ge(p_in, 16 * 9)
            nc.tensor.matmul(sps[:, 0:NS], w0s[:], condt[:], start=True, stop=True).then_inc(mm, 1)
            nc.tensor.matmul(gps[:, 0:NS], cwt[:], condt[:], start=True, stop=True)
            pe.wait_ge(gelu, 1)
            nc.tensor.matmul(sps[:, NS:2 * NS], w1s[:], h1[:], start=True, stop=True).then_inc(mm, 1)
            pe.wait_ge(gelu, 2)
            pe.wait_ge(zeroed, 1)
            nc.tensor.matmul(sps[:, 2 * NS:2 * NS + KE], h2[:], w2s[:], start=True, stop=False)
            nc.tensor.matmul(sps[:, 2 * NS:2 * NS + KE], ones[:], b2s[:], start=False, stop=True).then_inc(mm, 1)
            pe.wait_ge(sm, 3)
            pe.wait_ge(pw_in, 48)
            nc.tensor.matmul(sps[0:KE, 3 * NS:4 * NS], att[:], ident, start=True, stop=True).then_inc(mm, 1)
            pe.wait_ge(gelu, 4)
            pe.wait_ge(pm_in, 32)
            pe.wait_ge(b_act, 1)
            nc.tensor.matmul(gps[:, NS:2 * NS], bks[:], attt[:], start=True, stop=True).then_inc(mm, 1)
            for a in range(C // 4):
                if a >= G:
                    pe.wait_ge(agg_out, a - G + 1)
                for o in range(4):
                    last = nc.tensor.matmul(
                        yps[a % G][:, o // 2, o % 2 * NS:o % 2 * NS + NS], mixw[:, 4 * a + o], attt[:],
                        start=True, stop=True)
                last.then_inc(agg_mm, 1)
            pe.wait_ge(w_lo, 1)
            pe.wait_ge(agg_out, C // 4)

            def conv(n, slot, g):
                if g % 2 == 0:
                    pe.wait_ge(lo_made, 2 * n + g // 2 + 1)
                if not (isinstance(n, int) and n < 1):
                    pe.wait_ge(ycol_made, 4 * n - 3 + g)
                parts = [(wlo, xhi), (whi, xlo), (whi, xhi)]
                for i, (w, v) in enumerate(parts):
                    for b in range(2):
                        last = nc.tensor.matmul(yps[g][:].rearrange("p s (r j) -> p s r j", r=PR), w[:, b, g],
                                                v[slot][:, :, g, b:b + NJ].rearrange("p (r s) j -> p s r j", r=PR),
                                                start=i + b == 0, stop=i == 2 and b == 1)
                last.then_inc(conv_done, 1)

            def mix(n, slot, r):
                if r == 0:
                    pe.wait_ge(ynat_made, n + 1)
                pe.wait_ge(mixv_made, 2 * n + r + 1)
                if isinstance(n, int) and n + r < 1:
                    pe.wait_ge(b_act, 2)
                else:
                    pe.wait_ge(gam_made, 2 * n + r)
                nc.tensor.matmul(gps[:, 2 * slot + r:2 * slot + r + 1], mixv[slot][:, r], beta[:, 0, bass.ds(2 * n + r, 1)],
                                 start=True, stop=True).then_inc(gam_mm, 1)
                if not (isinstance(n, int) and n < 1 and r == 0):
                    pe.wait_ge(z_made, 2 * n + r)
                for h in range(2):
                    cut = slice(BANK * h, BANK * h + BANK)
                    last = nc.tensor.matmul(zps[:, cut], mixv[slot][:, r], ynat[slot][:, r, cut], start=True, stop=True)
                last.then_inc(mix_done, 1)

            def both(n, slot):
                conv(n, slot, 0)
                mix(n - 1, 1 - slot, 0)
                conv(n, slot, 1)
                conv(n, slot, 2)
                mix(n - 1, 1 - slot, 1)
                conv(n, slot, 3)

            for g in range(G):
                conv(0, 0, g)
            pe.wait_ge(b_dve, 4)
            both(1, 1)
            both(2, 0)
            with pe.Fori(1, NB // 2 - 1) as i:
                both(2 * i + 1, 1)
                both(2 * i + 2, 0)
            both(NB - 1, 1)
            mix(NB - 1, 1, 0)
            mix(NB - 1, 1, 1)


def constants():
    k, r = np.arange(P) // 32, np.arange(P) % 32
    phase, cc = r // CC, r % CC
    alike = (k[:, None] == k) & (cc[:, None] == cc)
    gap = phase[:, None] - phase
    residual = [alike & (gap == TAPS // 2), alike & (gap + PH == TAPS // 2)]
    c, s, g = np.arange(P) // SG, np.arange(P) // G % 2, np.arange(P) % G
    o = np.arange(C)
    same = (c[:, None] == o // G) & (g[:, None] == o % G)
    smask = s[:, None] == np.arange(2)
    ebits = -np.stack([phase < PAD, phase >= PAD], 1).astype(np.int32)
    return np.concatenate([*residual, np.eye(P) > 0, same, smask], 1).astype(np.float32), ebits


def rows(v):
    v = v.reshape(-1, G, CG).transpose(0, 2, 1)[:, :, None, :]
    return np.broadcast_to(v, (v.shape[0], CG, 2, G)).reshape(-1, P)


def conv_places(w):
    w = w.reshape(G, KQ, CC, KQ, CC, TAPS).transpose(3, 4, 0, 1, 2, 5)
    at = np.zeros((KQ, PH, CC, 2, G, KQ, PH, CC), w.dtype)
    for b in range(2):
        for p in range(PH):
            for q in range(PH):
                if 0 <= p - q + PH * b < TAPS:
                    at[:, p, :, b, :, :, q, :] = w[..., p - q + PH * b]
    return at.reshape(P, 2, G, P)


def kernel(**inputs):
    import concourse.bacc as bacc
    from concourse.bass_utils import run_bass_kernel_spmd

    a = {n: np.asarray(v) for n, v in inputs.items()}
    mix_w = a["L1_cond_weight"].reshape(KE, G, CG, C).transpose(0, 2, 1, 3).reshape(KE * C, C)
    consts, ebits = constants()
    arrays = {
        "x": a["x"], "cond_t": a["cond_128"].T, "cw_t": rows(a["L0_cond_c_weight"].T),
        "fside": rows(a["fside_S_0"]).T, "conv_w": conv_places(a["L0_cond_weight"]),
        "w0": a["L1_cond_W0"], "b0": a["L1_cond_b0"][:, None], "w1": a["L1_cond_W1"], "b1": a["L1_cond_b1"][:, None],
        "w2": a["L1_cond_W2"], "b2": a["L1_cond_b2"][None], "mix_w": rows(mix_w).reshape(KE, C, P),
        "bias_k": rows(a["L1_cond_bias_k"]), "consts": consts, "ebits": ebits,
    }
    arrays = {f"in_{n}": np.ascontiguousarray(v) for n, v in arrays.items()}
    nc = bacc.Bacc("TRN2", target_bir_lowering=False, num_devices=1)
    args = [nc.dram_tensor(n, v.shape, mybir.dt.from_np(v.dtype), kind="ExternalInput").ap() for n, v in arrays.items()]
    args.append(nc.dram_tensor("out", (NS, C, L), F32, kind="ExternalOutput").ap())
    build(nc, *args)
    r = run_bass_kernel_spmd(nc, [arrays], core_ids=[0])
    return r.results[0]["out"]
```

```python
from contextlib import ExitStack

import numpy as np

import concourse.bass as bass
from concourse import mybir

F32 = mybir.dt.float32
F32R = mybir.dt.float32r
I32 = mybir.dt.int32
ALU = mybir.AluOpType
ACT = mybir.ActivationFunctionType
AX = mybir.AxisListType

P = 128
NS, C, L = 128, 64, 1024
G, TAPS, PAD = 4, 9, 4
CG = C // G
KQ = 4
PH = 8
NJ = L // PH
JB = NJ // 32
CC = CG // KQ
SG = 2 * G
S = 4
NB = NS // S
PR = S // 2
NP = NS // 2
KE = 8
D = 128
XW = PAD + L
TJ = NJ + 1
BANK = 512
EX = 2 * KE + 1
AO = P // EX
AGG = -(-(C + 1) // AO)
AGG_OUT = [min(AO, C - AO * a) for a in range(AGG)]
MLP_PARTS = {"condt": NS, "w0": D, "w1": D, "w2": KE, "b0": 1, "b1": 1, "fside": 1,
             "smask": 2,
             "parity": 2,
             "pairs": NP,
             "turn": AO,
             "ones": P, "b2": KE}
MLP_COLS = sum(MLP_PARTS.values())


def build(nc, x, conv_w, mlp, cond_w, mix_w, edge_bits, out):
    ctx = ExitStack()
    with ctx:
        def sb(name, shape, dt=F32):
            return ctx.enter_context(nc.sbuf_tensor(name, shape, dt))

        def ps(name, shape):
            return ctx.enter_context(nc.psum_tensor(name, shape, F32))

        def sem(name):
            return ctx.enter_context(nc.semaphore(name))

        xin = [sb(f"xin{i}", [P, PR, XW]) for i in range(2)]
        xcol = sb("xcol", [P, PR * JB, PH, CC * SG])
        xph = [sb(f"xph{i}", [P, S, G, TJ]) for i in range(2)]
        xhi = [sb(f"xhi{i}", [P, S, G, TJ], F32R) for i in range(2)]
        xlo = [sb(f"xlo{i}", [P, S, G, TJ], F32R) for i in range(2)]
        ycol = sb("ycol", [P, PR * JB, PH * CC, 2, G])
        ynat = [sb(f"ynat{i}", [P, PR, L]) for i in range(2)]
        zout = [sb(f"zout{i}", [P, PR, L]) for i in range(2)]
        mixt = sb("mixt", [P, CG, G, NP])
        mixv = [sb(f"mixv{i}", [P, PR, P]) for i in range(2)]
        wraw = sb("wraw", [P, 2 * G + 2, P])
        whi = sb("whi", [P, 2, G, P], F32R)
        wlo = sb("wlo", [P, 2, G, P], F32R)
        wsum = wraw[:, 0:2 * G].rearrange("p (b g) c -> p b g c", b=2)
        residual = wraw[:, 2 * G:]
        mixw = sb("mixw", [AO * EX, AGG, P])
        mlps = sb("mlps", [P, MLP_COLS])
        cut = dict(zip(MLP_PARTS, np.cumsum([0, *MLP_PARTS.values()])))
        condt, w0s, w1s, w2s, b0s, b1s, fsides, smask, parity, pairs, turn, ones, b2s = (
            mlps[:, cut[n]:cut[n] + MLP_PARTS[n]] for n in MLP_PARTS)
        cws = sb("cws", [P, 2, P])
        ebits = sb("ebits", [P, 2], I32)
        h1, h2 = sb("h1", [P, NS]), sb("h2", [P, NS])
        negmax, esum, erec = sb("negmax", [P, 1]), sb("esum", [P, 1]), sb("erec", [P, 1])
        expv = sb("expv", [P, KE])
        att = sb("att", [P, AO, EX])
        attt = sb("attt", [AO * EX, AO, NP])
        beta = sb("beta", [P, 2, NP])
        gam = [sb(f"gam{i}", [P, PR]) for i in range(2)]

        yps = [ps(f"yps{g}", [P, 2, PR * NJ]) for g in range(G)]
        zps = ps("zps", [P, L])
        gps = ps("gps", [P, BANK])
        sps = ps("sps", [P, BANK])

        x_in = [sem(f"x_in{i}") for i in range(2)]
        x_first = sem("x_first")
        z_out = [sem(f"z_out{i}") for i in range(2)]
        mlp_in, cw_in, w_in, e_in, mix_in = (sem(n) for n in (
            "mlp_in", "cw_in", "w_in", "e_in", "mix_in"))
        wrapped_0 = sem("wrapped_0")
        wrapped = sem("wrapped")
        cols_made = sem("cols_made")
        turned = sem("turned")
        edged = sem("edged")
        hi_made = sem("hi_made")
        lo_made = sem("lo_made")
        conv_done = sem("conv_done")
        ycol_made = sem("ycol_made")
        ynat_made = sem("ynat_made")
        mixv_made = sem("mixv_made")
        gam_mm = sem("gam_mm")
        gam_made = sem("gam_made")
        mix_done = sem("mix_done")
        z_made = sem("z_made")
        w_sum = sem("w_sum")
        w_hi, w_lo = sem("w_hi"), sem("w_lo")
        mm = sem("mm")
        act_mlp = sem("act_mlp")
        soft = sem("soft")
        beta_mm = sem("beta_mm")
        beta_made = sem("beta_made")
        agg_mm = sem("agg_mm")
        agg_out = sem("agg_out")

        def x_rows(t, pair):
            return t.rearrange("(n s) (g c) l -> n c (s g) l", s=2, g=G)[bass.ds(pair, 1)].rearrange(
                "n c q l -> (n c) q l")

        block = ctx.enter_context(nc.Block())

        @block.sync
        def _(sp):
            def load(n, slot):
                if not (isinstance(n, int) and n < 2):
                    sp.wait_ge(cols_made, 2 * n - 2)
                for r in range(PR):
                    sp.dma_start(xin[slot][:, r, PAD:], x_rows(x, 2 * n + r)).then_inc(x_in[slot], 16)

            def store(n, slot):
                for r in range(PR):
                    sp.wait_ge(z_made, 2 * n + r + 1)
                    sp.dma_start(x_rows(out, 2 * n + r), zout[slot][:, r]).then_inc(z_out[slot], 16)

            for r in range(PR):
                sp.dma_start(xin[0][:, r, PAD:], x_rows(x, r)).then_inc((x_first, x_in[0])[r], 16)
            sp.dma_start(mlps[:], mlp).then_inc(mlp_in, 16)
            sp.dma_start(wraw[:], conv_w).then_inc(w_in, 16)
            load(1, 1)
            sp.dma_start(cws[:], cond_w).then_inc(cw_in, 16)
            sp.dma_start(mixw[:], mix_w).then_inc(mix_in, 16)
            for n in range(2, 6):
                load(n, n % 2)
            with sp.Fori(0, NB // 2 - 3) as i:
                for c in range(2):
                    load(2 * i + c + 6, c)
                    store(2 * i + c, c)
            for n in range(NB - 6, NB):
                store(n, n % 2)
            for slot in range(2):
                sp.wait_ge(z_out[slot], 32 * (NB // 2))

        @block.gpsimd
        def _(pool):
            def low(n, slot):
                for h in range(2):
                    pool.wait_ge(hi_made, 2 * n + h + 1)
                    g = slice(2 * h, 2 * h + 2)
                    nc.gpsimd.tensor_tensor(xlo[slot][:, :, g], xph[slot][:, :, g], xhi[slot][:, :, g].bitcast(F32),
                                            ALU.subtract).then_inc(lo_made, 1)

            def matrices(n, slot):
                if not (isinstance(n, int) and n < 2):
                    pool.wait_ge(mix_done, 2 * n - 2)
                for r in range(PR):
                    nc.gpsimd.tensor_tensor(
                        mixv[slot][:, r].rearrange("p (c s g) -> p c s g", c=CG, s=2),
                        mixt[:, :, :, bass.ds(2 * n + r, 1)].rearrange("p c g o -> p c o g").broadcast_to([P, CG, 2, G]),
                        smask.unsqueeze(1).unsqueeze(3).broadcast_to([P, CG, 2, G]),
                        ALU.mult).then_inc(mixv_made, 1)

            for r in range(PR):
                pool.wait_ge((x_first, x_in[0])[r], 16)
                nc.gpsimd.tensor_copy(xin[0][:, r, 0:PAD], xin[0][:, r, L:]).then_inc(wrapped_0, 1)
            pool.wait_ge(w_hi, 1)
            nc.gpsimd.tensor_tensor(wlo[:], wsum, whi[:].bitcast(F32), ALU.subtract).then_inc(w_lo, 1)
            low(0, 0)
            low(1, 1)
            low(2, 0)
            pool.wait_ge(agg_out, AGG)
            matrices(0, 0)
            for n in range(2):
                low(n + 3, 1 - n)
                matrices(n + 1, 1 - n)
            with pool.Fori(1, NB // 2 - 3) as i:
                for c in range(2):
                    low(2 * i + c + 3, 1 - c)
                    matrices(2 * i + c + 1, 1 - c)
            low(NB - 3, 1)
            matrices(NB - 5, 1)
            low(NB - 2, 0)
            matrices(NB - 4, 0)
            low(NB - 1, 1)
            matrices(NB - 3, 1)
            matrices(NB - 2, 0)
            matrices(NB - 1, 1)

        @block.scalar
        def _(act):
            act.dma_start(ebits[:], edge_bits).then_inc(e_in, 16)

            def wrap(n, slot):
                act.wait_ge(x_in[slot], 16 * n + 16)
                nc.scalar.activation(xin[slot][:, :, 0:PAD], xin[slot][:, :, L:], ACT.Copy).then_inc(wrapped, 1)

            def high(n, slot):
                act.wait_ge(edged, n + 1)
                for h in range(2):
                    if not (isinstance(n, int) and n < 2):
                        act.wait_ge(conv_done, 4 * n - 6 + 2 * h)
                    g = slice(2 * h, 2 * h + 2)
                    nc.scalar.activation(xhi[slot][:, :, g], xph[slot][:, :, g], ACT.Copy).then_inc(hi_made, 1)

            def evacuate(n, slot):
                for r in range(PR):
                    act.wait_ge(gam_mm, 2 * n + r + 1)
                    nc.scalar.activation(gam[slot][:, r:r + 1], gps[:, 2 * slot + r:2 * slot + r + 1], ACT.Identity,
                                         bias=beta[:, 1, bass.ds(2 * n + r, 1)]).then_inc(gam_made, 1)
                    act.wait_ge(gam_made, 2 * n + r + 1)
                    act.wait_ge(mix_done, 2 * n + r + 1)
                    if r == 0 and not (isinstance(n, int) and n < 2):
                        act.wait_ge(z_out[slot], 32 * (n // 2) if isinstance(n, int) else 16 * n - 16 * slot)
                    nc.scalar.activation(
                        zout[slot][:, r].rearrange("p (b j q) -> p b q j", b=JB, q=PH),
                        zps[:].rearrange("p (b q j) -> p b q j", b=JB, q=PH), ACT.Identity,
                        bias=gam[slot][:, r:r + 1]).then_inc(z_made, 1)

            def gather(a):
                act.wait_ge(agg_mm, a + 1)
                nc.scalar.activation(mixt[:].rearrange("p c g b -> p (c g b)")[:, AO * NP * a:AO * NP * a + NP * AGG_OUT[a]],
                                     zps[:, BANK * (a % 2):BANK * (a % 2) + NP * AGG_OUT[a]], ACT.Copy).then_inc(agg_out, 1)

            act.wait_ge(mlp_in, 16)
            act.wait_ge(mm, 1)
            nc.scalar.activation(h1[:], sps[:, 0:NS], ACT.Gelu, bias=b0s).then_inc(act_mlp, 1)
            act.wait_ge(mm, 2)
            nc.scalar.activation(h2[:], sps[:, NS:2 * NS], ACT.Gelu, bias=b1s).then_inc(act_mlp, 1)
            act.wait_ge(w_sum, 1)
            nc.scalar.activation(whi[:], wsum, ACT.Copy).then_inc(w_hi, 1)
            act.wait_ge(soft, 1)
            nc.scalar.activation(expv[:], sps[:, 2 * NS:2 * NS + KE], ACT.Exp, bias=negmax[:],
                                 accum_out=esum[:]).then_inc(act_mlp, 1)
            wrap(1, 1)
            high(0, 0)
            wrap(2, 0)
            high(1, 1)
            act.wait_ge(beta_mm, 1)
            nc.scalar.activation(beta[:, 0], gps[:, NP:2 * NP], ACT.Identity, bias=fsides).then_inc(beta_made, 1)
            wrap(3, 1)
            for a in range(4):
                gather(a)
            high(2, 0)
            for a in range(4, 6):
                gather(a)
            wrap(4, 0)
            for a in range(6, AGG):
                gather(a)
            last = BANK * ((AGG - 1) % 2) + NP * AGG_OUT[-1]
            nc.scalar.activation(beta[:, 1], zps[:, last:last + NP], ACT.Copy).then_inc(beta_made, 1)
            high(3, 1)
            act.wait_ge(beta_made, 2)

            def around(n, slot):
                wrap(n + 5, 1 - slot)
                evacuate(n, slot)
                high(n + 4, slot)

            for n in range(2):
                around(n, n)
            with act.Fori(1, NB // 2 - 3) as i:
                for c in range(2):
                    around(2 * i + c, c)
            around(NB - 6, 0)
            evacuate(NB - 5, 1)
            high(NB - 1, 1)
            for n in range(NB - 4, NB):
                evacuate(n, n % 2)

        @block.vector
        def _(dve):
            def columns(n, slot):
                if not (isinstance(n, int) and n < 1):
                    dve.wait_ge(wrapped, n)
                if not (isinstance(n, int) and n < 1):
                    dve.wait_ge(turned, 2 * n)
                for r in range(PR):
                    if isinstance(n, int) and n < 1:
                        dve.wait_ge(wrapped_0, r + 1)
                    nc.vector.transpose(
                        xcol[:, JB * r:JB * r + JB].rearrange("q b p c -> q (b p c)"),
                        xin[slot][:, r, 0:L].rearrange("q (b j p) -> q b p j", j=32, p=PH)).then_inc(cols_made, 1)

            def phases(n, slot, r):
                if r == 0:
                    dve.wait_ge(cols_made, 2 * n + 2)
                    if not (isinstance(n, int) and n < 2):
                        dve.wait_ge(lo_made, 2 * n - 2)
                nc.vector.transpose(
                    xph[slot][:, 2 * r:2 * r + 2, :, 0:NJ].rearrange("q s g (b j) -> q b (s g) j", j=32),
                    xcol[:, JB * r:JB * r + JB].rearrange("q b p (c h) -> q b h (p c)", c=CC)).then_inc(turned, 1)

            def edges(n, slot):
                v = xph[slot][:].bitcast(I32).rearrange("q s g j -> q j (s g)")
                dve.wait_ge(turned, 2 * n + 2)
                nc.vector.tensor_tensor(v[:, NJ::-NJ], v[:, 0:1].broadcast_to([P, 2, S * G]),
                                        ebits[:].unsqueeze(2).broadcast_to([P, 2, S * G]),
                                        ALU.bitwise_and).then_inc(edged, 1)

            def y_columns(n, g):
                dve.wait_ge(conv_done, 4 * n + g + 1)
                if g == 0 and not (isinstance(n, int) and n < 1):
                    dve.wait_ge(ynat_made, n)
                nc.vector.transpose(ycol[:, :, :, :, g].rearrange("q b c s -> q s b c"),
                                    yps[g][:].rearrange("q s (b j) -> q s b j", j=32)).then_inc(ycol_made, 1)

            def y_natural(n, slot):
                dve.wait_ge(ycol_made, 4 * n + 4)
                if not (isinstance(n, int) and n < 2):
                    dve.wait_ge(mix_done, 2 * n - 2)
                nc.vector.transpose(ynat[slot].rearrange("q r c -> q (r c)"),
                                    ycol[:].rearrange("q b c s g -> q (b c s g)")).then_inc(ynat_made, 1)

            def ahead(n, slot):
                columns(n, slot)
                phases(n, slot, 0)
                phases(n, slot, 1)
                edges(n, slot)

            dve.wait_ge(e_in, 16)
            ahead(0, 0)
            dve.wait_ge(w_in, 16)
            nc.vector.tensor_tensor(wsum, wsum, residual.unsqueeze(2).broadcast_to([P, 2, G, P]),
                                    ALU.add).then_inc(w_sum, 1)
            dve.wait_ge(mm, 3)
            nc.vector.tensor_reduce(negmax[:], sps[:, 2 * NS:2 * NS + KE], AX.X, ALU.max, negate=True).then_inc(soft, 1)
            dve.wait_ge(act_mlp, 3)
            nc.vector.reciprocal(erec[:], esum[:]).then_inc(soft, 1)
            nc.vector.tensor_copy(att[:, :, 2 * KE], parity[:, 0:1].broadcast_to([P, AO])).then_inc(soft, 1)
            dve.wait_ge(soft, 2)
            for k in range(2):
                nc.vector.tensor_scalar(att[:, :, KE * k:KE * k + KE], expv[:].unsqueeze(1).broadcast_to([P, AO, KE]),
                                        erec[:], parity[:, k:k + 1], ALU.mult, ALU.mult).then_inc(soft, 1)
            columns(1, 1)
            dve.wait_ge(mm, 4)
            nc.vector.tensor_tensor(attt[:], sps[0:AO * EX, 3 * NS:3 * NS + NP].unsqueeze(1).broadcast_to([AO * EX, AO, NP]),
                                    turn[0:AO * EX].unsqueeze(2).broadcast_to([AO * EX, AO, NP]), ALU.mult).then_inc(soft, 1)
            phases(1, 1, 0)
            phases(1, 1, 1)
            edges(1, 1)
            ahead(2, 0)

            def step(n, slot, more=True):
                if more:
                    columns(n + 3, 1 - slot)
                y_columns(n, 0)
                if more:
                    phases(n + 3, 1 - slot, 0)
                y_columns(n, 1)
                if more:
                    phases(n + 3, 1 - slot, 1)
                y_columns(n, 2)
                y_columns(n, 3)
                if more:
                    edges(n + 3, 1 - slot)
                y_natural(n, slot)

            for n in range(2):
                step(n, n)
            with dve.Fori(1, NB // 2 - 2) as i:
                for c in range(2):
                    step(2 * i + c, c)
            step(NB - 4, 0)
            for n in range(NB - 3, NB):
                step(n, n % 2, more=False)

        @block.tensor
        def _(pe):
            pe.wait_ge(mlp_in, 16)
            nc.tensor.matmul(sps[:, 0:NS], w0s, condt, start=True, stop=True).then_inc(mm, 1)
            pe.wait_ge(act_mlp, 1)
            nc.tensor.matmul(sps[:, NS:2 * NS], w1s, h1[:], start=True, stop=True).then_inc(mm, 1)
            pe.wait_ge(act_mlp, 2)
            nc.tensor.matmul(sps[:, 2 * NS:2 * NS + KE], h2[:], w2s, start=True, stop=False)
            nc.tensor.matmul(sps[:, 2 * NS:2 * NS + KE], ones[0:1], b2s[0:1], start=False, stop=True).then_inc(mm, 1)
            pe.wait_ge(cw_in, 16)
            for k in range(2):
                last = nc.tensor.matmul(gps[:, NP:2 * NP], cws[:, k], condt[:, k::2], start=k == 0, stop=k == 1)
            last.then_inc(beta_mm, 1)
            pe.wait_ge(soft, 5)
            nc.tensor.matmul(sps[0:AO * EX, 3 * NS:3 * NS + NP], att[:].rearrange("p o e -> p (o e)"), pairs, start=True, stop=True).then_inc(mm, 1)
            pe.wait_ge(soft, 6)
            pe.wait_ge(mix_in, 16)

            def aggregate(a):
                if a >= 2:
                    pe.wait_ge(agg_out, a - 1)
                n = min(AO, C + 1 - AO * a)
                nc.tensor.matmul(zps[:, BANK * (a % 2):BANK * (a % 2) + NP * n].rearrange("p (o b) -> p o b", o=n),
                                 mixw[:, a], attt[:, 0:n], start=True, stop=True).then_inc(agg_mm, 1)

            def conv(n, slot, g):
                if g % 2 == 0:
                    pe.wait_ge(lo_made, 2 * n + g // 2 + 1)
                if not (isinstance(n, int) and n < 1):
                    pe.wait_ge(ycol_made, 4 * n - 3 + g)
                parts = [(wlo, xhi), (whi, xlo), (whi, xhi)]
                for i, (w, v) in enumerate(parts):
                    for b in range(2):
                        last = nc.tensor.matmul(yps[g][:].rearrange("p s (r j) -> p s r j", r=PR), w[:, b, g],
                                                v[slot][:, :, g, b:b + NJ].rearrange("p (r s) j -> p s r j", r=PR),
                                                start=i + b == 0, stop=i == 2 and b == 1)
                last.then_inc(conv_done, 1)

            def mix(n, slot, r):
                if r == 0:
                    pe.wait_ge(ynat_made, n + 1)
                pe.wait_ge(mixv_made, 2 * n + r + 1)
                if isinstance(n, int) and n + r < 1:
                    pe.wait_ge(beta_made, 2)
                else:
                    pe.wait_ge(gam_made, 2 * n + r)
                nc.tensor.matmul(gps[:, 2 * slot + r:2 * slot + r + 1], mixv[slot][:, r], beta[:, 0, bass.ds(2 * n + r, 1)],
                                 start=True, stop=True).then_inc(gam_mm, 1)
                if not (isinstance(n, int) and n < 1 and r == 0):
                    pe.wait_ge(z_made, 2 * n + r)
                for h in range(2):
                    bank = slice(BANK * h, BANK * h + BANK)
                    last = nc.tensor.matmul(zps[:, bank], mixv[slot][:, r], ynat[slot][:, r, bank], start=True, stop=True)
                last.then_inc(mix_done, 1)

            def both(n, slot):
                mix(n - 2, slot, 0)
                conv(n, slot, 0)
                conv(n, slot, 1)
                mix(n - 2, slot, 1)
                conv(n, slot, 2)
                conv(n, slot, 3)

            pe.wait_ge(w_lo, 1)
            for g in range(G):
                conv(0, 0, g)
            for a in range(6):
                aggregate(a)
            conv(1, 1, 0)
            for a in range(6, AGG):
                aggregate(a)
            for g in range(1, G):
                conv(1, 1, g)
            both(2, 0)
            both(3, 1)
            with pe.Fori(2, NB // 2) as i:
                both(2 * i, 0)
                both(2 * i + 1, 1)
            for n in range(NB - 2, NB):
                for r in range(PR):
                    mix(n, n % 2, r)


def constants():
    k, r = np.arange(P) // 32, np.arange(P) % 32
    phase, cc = r // CC, r % CC
    alike = (k[:, None] == k) & (cc[:, None] == cc)
    gap = phase[:, None] - phase
    residual = np.stack([alike & (gap == TAPS // 2), alike & (gap + PH == TAPS // 2)], 1)
    s = np.arange(P) // G % 2
    smask = s[:, None] == np.arange(2)
    parity = np.arange(NS)[:, None] % 2 == np.arange(2)
    pairs = np.arange(NS)[:, None] // 2 == np.arange(NP)
    turn = np.arange(P)[:, None] // EX == np.arange(AO)
    ebits = -np.stack([phase < PAD, phase >= PAD], 1).astype(np.int32)
    return residual.astype(np.float32), smask, parity, pairs, turn, ebits


def rows(v):
    v = v.reshape(-1, G, CG).transpose(0, 2, 1)[:, :, None, :]
    return np.broadcast_to(v, (v.shape[0], CG, 2, G)).reshape(-1, P)


def by_sample(v):
    s = np.arange(P) // G % 2
    return np.stack([np.where(s == k, v, np.zeros_like(v)) for k in range(2)])


def conv_places(w):
    w = w.reshape(G, KQ, CC, KQ, CC, TAPS).transpose(3, 4, 0, 1, 2, 5)
    at = np.zeros((KQ, PH, CC, 2, G, KQ, PH, CC), w.dtype)
    for b in range(2):
        for p in range(PH):
            for q in range(PH):
                if 0 <= p - q + PH * b < TAPS:
                    at[:, p, :, b, :, :, q, :] = w[..., p - q + PH * b]
    return at.reshape(P, 2 * G, P)


def kernel(**inputs):
    import concourse.bacc as bacc
    from concourse.bass_utils import run_bass_kernel_spmd

    a = {n: np.asarray(v) for n, v in inputs.items()}
    residual, smask, parity, pairs, turn, ebits = constants()
    out_c = a["L1_cond_weight"].reshape(KE, G, CG, C).transpose(0, 2, 1, 3).reshape(KE * C, C)
    mix_w = by_sample(rows(out_c).reshape(KE, C, P))
    bias_k = by_sample(rows(a["L1_cond_bias_k"]))[:, :, None]
    same = rows(np.eye(C, dtype=np.float32).reshape(G, CG, C).transpose(1, 0, 2).reshape(C, C))
    experts = np.concatenate([mix_w, bias_k], 2).reshape(2 * KE, C + 1, P)
    identity = np.concatenate([same, np.zeros((1, P), np.float32)])[None]
    mix_w = np.zeros((EX, AGG * AO, P), np.float32)
    mix_w[:, :C + 1] = np.concatenate([experts, identity])
    mix_w = mix_w.reshape(EX, AGG, AO, P).transpose(2, 0, 1, 3).reshape(AO * EX, AGG, P)
    mlp = np.zeros((P, MLP_COLS), np.float32)
    at = 0
    for name, v in {
            "condt": a["cond_128"].T, "w0": a["L1_cond_W0"], "w1": a["L1_cond_W1"], "w2": a["L1_cond_W2"],
            "b0": a["L1_cond_b0"][:, None], "b1": a["L1_cond_b1"][:, None], "fside": rows(a["fside_S_0"]).T,
            "smask": smask, "parity": parity, "pairs": pairs, "turn": turn, "ones": np.ones((1, P)), "b2": a["L1_cond_b2"][None]}.items():
        mlp[:len(v), at:at + MLP_PARTS[name]] = v
        at += MLP_PARTS[name]
    arrays = {
        "x": a["x"], "conv_w": np.concatenate([conv_places(a["L0_cond_weight"]), residual], 1), "mlp": mlp,
        "cond_w": by_sample(rows(a["L0_cond_c_weight"].T)).transpose(1, 0, 2),
        "mix_w": mix_w, "ebits": ebits,
    }
    arrays = {f"in_{n}": np.ascontiguousarray(v) for n, v in arrays.items()}
    nc = bacc.Bacc("TRN2", target_bir_lowering=False, num_devices=1)
    args = [nc.dram_tensor(n, v.shape, mybir.dt.from_np(v.dtype), kind="ExternalInput").ap() for n, v in arrays.items()]
    args.append(nc.dram_tensor("out", (NS, C, L), F32, kind="ExternalOutput").ap())
    build(nc, *args)
    r = run_bass_kernel_spmd(nc, [arrays], core_ids=[0])
    return r.results[0]["out"]
```

```python
from contextlib import ExitStack

import numpy as np

import concourse.bass as bass
from concourse import mybir

F32 = mybir.dt.float32
F32R = mybir.dt.float32r
I32 = mybir.dt.int32
ALU = mybir.AluOpType
ACT = mybir.ActivationFunctionType
AX = mybir.AxisListType

P = 128
NS, C, L = 128, 64, 1024
G, TAPS, PAD = 4, 9, 4
CG = C // G
KQ = 4
PH = 8
NJ = L // PH
JB = NJ // 32
CC = CG // KQ
SG = 2 * G
S = 4
NB = NS // S
PR = S // 2
NP = NS // 2
KE = 8
D = 128
XW = PAD + L
TJ = NJ + 1
BANK = 512
EX = 2 * KE + 1
AO = P // EX
AGG = -(-(C + 1) // AO)
AGG_OUT = [min(AO, C - AO * a) for a in range(AGG)]
MLP_PARTS = {"condt": NS, "w0": D, "w1": D, "w2": KE, "b0": 1, "b1": 1, "fside": 1,
             "smask": 2,
             "parity": 2,
             "pairs": NP,
             "turn": AO,
             "ones": P, "b2": KE}
MLP_COLS = sum(MLP_PARTS.values())


def build(nc, x, conv_w, mlp, cond_w, mix_w, edge_bits, out):
    ctx = ExitStack()
    with ctx:
        def sb(name, shape, dt=F32):
            return ctx.enter_context(nc.sbuf_tensor(name, shape, dt))

        def ps(name, shape):
            return ctx.enter_context(nc.psum_tensor(name, shape, F32))

        def sem(name):
            return ctx.enter_context(nc.semaphore(name))

        xin = [sb(f"xin{i}", [P, PR, XW]) for i in range(2)]
        xcol = sb("xcol", [P, JB, PH, CC, PR, SG])
        xph = [sb(f"xph{i}", [P, S, G, TJ]) for i in range(2)]
        xhi = [sb(f"xhi{i}", [P, S, G, TJ], F32R) for i in range(2)]
        xlo = [sb(f"xlo{i}", [P, S, G, TJ], F32R) for i in range(2)]
        ycol = sb("ycol", [P, PR * JB, PH * CC, 2, G])
        ynat = [sb(f"ynat{i}", [P, PR, L]) for i in range(2)]
        zout = [sb(f"zout{i}", [P, PR, L]) for i in range(2)]
        mixt = sb("mixt", [P, CG, G, NP])
        mixv = [sb(f"mixv{i}", [P, PR, P]) for i in range(2)]
        wraw = sb("wraw", [P, 2 * G + 2, P])
        whi = sb("whi", [P, 2, G, P], F32R)
        wlo = sb("wlo", [P, 2, G, P], F32R)
        wsum = wraw[:, 0:2 * G].rearrange("p (b g) c -> p b g c", b=2)
        residual = wraw[:, 2 * G:]
        mixw = sb("mixw", [AO * EX, AGG, P])
        mlps = sb("mlps", [P, MLP_COLS])
        cut = dict(zip(MLP_PARTS, np.cumsum([0, *MLP_PARTS.values()])))
        condt, w0s, w1s, w2s, b0s, b1s, fsides, smask, parity, pairs, turn, ones, b2s = (
            mlps[:, cut[n]:cut[n] + MLP_PARTS[n]] for n in MLP_PARTS)
        cws = sb("cws", [P, 2, P])
        ebits = sb("ebits", [P, 2], I32)
        warm = sb("warm", [P, 1])
        h1, h2 = sb("h1", [P, NS]), sb("h2", [P, NS])
        negmax, esum, erec = sb("negmax", [P, 1]), sb("esum", [P, 1]), sb("erec", [P, 1])
        expv = sb("expv", [P, KE])
        att = sb("att", [P, AO, EX])
        attt = sb("attt", [AO * EX, AO, NP])
        beta = sb("beta", [P, 2, NP])
        gam = [sb(f"gam{i}", [P, PR]) for i in range(2)]

        yps = [ps(f"yps{g}", [P, 2, PR * NJ]) for g in range(G)]
        zps = ps("zps", [P, L])
        gps = ps("gps", [P, BANK])
        sps = ps("sps", [P, BANK])

        x_in = [sem(f"x_in{i}") for i in range(2)]
        x_first = sem("x_first")
        z_out = [sem(f"z_out{i}") for i in range(2)]
        mlp_in, cw_in, w_in, e_in, mix_in = (sem(n) for n in (
            "mlp_in", "cw_in", "w_in", "e_in", "mix_in"))
        wrapped_0 = sem("wrapped_0")
        wrapped = sem("wrapped")
        cols_made = sem("cols_made")
        turned = sem("turned")
        edged = sem("edged")
        hi_made = sem("hi_made")
        lo_made = sem("lo_made")
        conv_done = sem("conv_done")
        ycol_made = sem("ycol_made")
        ynat_made = sem("ynat_made")
        mixv_made = sem("mixv_made")
        gam_mm = sem("gam_mm")
        gam_made = sem("gam_made")
        mix_done = sem("mix_done")
        z_made = sem("z_made")
        zeroed = sem("zeroed")
        w_sum = sem("w_sum")
        w_hi, w_lo = sem("w_hi"), sem("w_lo")
        mm = sem("mm")
        act_mlp = sem("act_mlp")
        soft = sem("soft")
        beta_mm = sem("beta_mm")
        beta_made = sem("beta_made")
        agg_mm = sem("agg_mm")
        agg_out = sem("agg_out")

        def x_rows(t, pair):
            return t.rearrange("(n s) (g c) l -> n c (s g) l", s=2, g=G)[bass.ds(pair, 1)].rearrange(
                "n c q l -> (n c) q l")

        def yflat(g):
            return yps[g][:].rearrange("p s j -> p (s j)")

        block = ctx.enter_context(nc.Block())

        @block.sync
        def _(sp):
            def load(n, slot):
                if not (isinstance(n, int) and n < 2):
                    sp.wait_ge(cols_made, 2 * n - 2)
                for r in range(PR):
                    sp.dma_start(xin[slot][:, r, PAD:], x_rows(x, 2 * n + r)).then_inc(x_in[slot], 16)

            def store(n, slot, pairs=range(PR)):
                for r in pairs:
                    sp.wait_ge(z_made, 2 * n + r + 1)
                    sp.dma_start(x_rows(out, 2 * n + r), zout[slot][:, r]).then_inc(z_out[slot], 16)

            for r in range(PR):
                sp.dma_start(xin[0][:, r, PAD:], x_rows(x, r)).then_inc((x_first, x_in[0])[r], 16)
            sp.dma_start(mlps[:], mlp).then_inc(mlp_in, 16)
            sp.dma_start(wraw[:], conv_w).then_inc(w_in, 16)
            load(1, 1)
            sp.dma_start(cws[:], cond_w).then_inc(cw_in, 16)
            sp.dma_start(mixw[:], mix_w).then_inc(mix_in, 16)
            for n in range(2, 6):
                load(n, n % 2)
            store(0, 0)
            with sp.Fori(1, NB // 2 - 2) as i:
                for c in range(2):
                    load(2 * i + c + 4, c)
                    store(2 * i + c - 1, 1 - c)
            for n in range(NB - 5, NB - 1):
                store(n, n % 2)
            store(NB - 1, 1, [0])
            for h in range(2):
                sp.wait_ge(z_made, 2 * NB + h)
                sp.dma_start(x_rows(out, NP - 1)[:, :, BANK * h:BANK * h + BANK],
                             zout[1][:, 1, BANK * h:BANK * h + BANK]).then_inc(z_out[1], 16)
            for slot in range(2):
                sp.wait_ge(z_out[slot], 32 * (NB // 2) + 16 * slot)

        @block.gpsimd
        def _(pool):
            def low(n, slot):
                for h in range(2):
                    pool.wait_ge(hi_made, 2 * n + h + 1)
                    g = slice(2 * h, 2 * h + 2)
                    nc.gpsimd.tensor_tensor(xlo[slot][:, :, g], xph[slot][:, :, g], xhi[slot][:, :, g].bitcast(F32),
                                            ALU.subtract).then_inc(lo_made, 1)

            def matrices(n, slot):
                if not (isinstance(n, int) and n < 2):
                    pool.wait_ge(mix_done, 2 * n - 2)
                for r in range(PR):
                    nc.gpsimd.tensor_tensor(
                        mixv[slot][:, r].rearrange("p (c s g) -> p c s g", c=CG, s=2),
                        mixt[:, :, :, bass.ds(2 * n + r, 1)].rearrange("p c g o -> p c o g").broadcast_to([P, CG, 2, G]),
                        smask.unsqueeze(1).unsqueeze(3).broadcast_to([P, CG, 2, G]),
                        ALU.mult).then_inc(mixv_made, 1)

            nc.gpsimd.memset(warm[:], 0.0).then_inc(zeroed, 1)
            for r in range(PR):
                pool.wait_ge((x_first, x_in[0])[r], 16)
                nc.gpsimd.tensor_copy(xin[0][:, r, 0:PAD], xin[0][:, r, L:]).then_inc(wrapped_0, 1)
            low(0, 0)
            low(1, 1)
            pool.wait_ge(agg_out, AGG)
            matrices(0, 0)
            low(2, 0)
            matrices(1, 1)
            with pool.Fori(1, NB // 2 - 1) as i:
                for c in range(2):
                    low(2 * i + c + 1, 1 - c)
                    matrices(2 * i + c, c)
            low(NB - 1, 1)
            matrices(NB - 2, 0)
            matrices(NB - 1, 1)

        @block.scalar
        def _(act):
            def wrap(n, slot):
                act.wait_ge(x_in[slot], 16 * n + 16)
                nc.scalar.activation(xin[slot][:, :, 0:PAD], xin[slot][:, :, L:], ACT.Copy).then_inc(wrapped, 1)

            def high(n, slot, halves=range(2)):
                act.wait_ge(edged, n + 1)
                for h in halves:
                    if not (isinstance(n, int) and n < 2):
                        act.wait_ge(conv_done, 4 * n - 6 + 2 * h)
                    g = slice(2 * h, 2 * h + 2)
                    nc.scalar.activation(xhi[slot][:, :, g], xph[slot][:, :, g], ACT.Copy).then_inc(hi_made, 1)

            def bias(n, slot, r):
                act.wait_ge(gam_mm, 2 * n + r + 1)
                nc.scalar.activation(gam[slot][:, r:r + 1], gps[:, 2 * slot + r:2 * slot + r + 1], ACT.Identity,
                                     bias=beta[:, 1, bass.ds(2 * n + r, 1)]).then_inc(gam_made, 1)
                act.wait_ge(gam_made, 2 * n + r + 1)

            def place(slot, r, at, product):
                size = product.shape[1]
                return nc.scalar.activation(
                    zout[slot][:, r, at:at + size].rearrange("p (b j q) -> p b q j", j=32, q=PH),
                    product.rearrange("p (b q j) -> p b q j", j=32, q=PH), ACT.Identity, bias=gam[slot][:, r:r + 1])

            def evacuate(n, slot, pairs=range(PR)):
                for r in pairs:
                    bias(n, slot, r)
                    act.wait_ge(mix_done, 2 * n + r + 1)
                    if r == 0 and not (isinstance(n, int) and n < 2):
                        act.wait_ge(z_out[slot], 32 * (n // 2) if isinstance(n, int) else 16 * n - 16 * slot)
                    place(slot, r, 0, zps[:]).then_inc(z_made, 1)

            def gather(a):
                act.wait_ge(agg_mm, a + 1)
                nc.scalar.activation(mixt[:].rearrange("p c g b -> p (c g b)")[:, AO * NP * a:AO * NP * a + NP * AGG_OUT[a]],
                                     zps[:, BANK * (a % 2):BANK * (a % 2) + NP * AGG_OUT[a]], ACT.Copy).then_inc(agg_out, 1)

            act.dma_start(ebits[:], edge_bits).then_inc(e_in, 16)
            act.wait_ge(zeroed, 1)
            nc.scalar.activation(warm[:], warm[:], ACT.Gelu)
            act.wait_ge(mlp_in, 16)
            act.wait_ge(mm, 1)
            nc.scalar.activation(h1[:], sps[:, 0:NS], ACT.Gelu, bias=b0s).then_inc(act_mlp, 1)
            act.wait_ge(mm, 2)
            nc.scalar.activation(h2[:], sps[:, NS:2 * NS], ACT.Gelu, bias=b1s).then_inc(act_mlp, 1)
            high(0, 0, [0])
            act.wait_ge(w_sum, 1)
            nc.scalar.activation(whi[:], wsum, ACT.Copy).then_inc(w_hi, 1)
            act.wait_ge(soft, 1)
            nc.scalar.activation(expv[:], sps[:, 2 * NS:2 * NS + KE], ACT.Exp, bias=negmax[:],
                                 accum_out=esum[:]).then_inc(act_mlp, 1)
            wrap(1, 1)
            high(0, 0, [1])
            wrap(2, 0)
            high(1, 1)
            act.wait_ge(beta_mm, 1)
            nc.scalar.activation(beta[:, 0], gps[:, NP:2 * NP], ACT.Identity, bias=fsides).then_inc(beta_made, 1)
            wrap(3, 1)
            for a in range(AGG):
                gather(a)
            last = BANK * ((AGG - 1) % 2) + NP * AGG_OUT[-1]
            nc.scalar.activation(beta[:, 1], zps[:, last:last + NP], ACT.Copy).then_inc(beta_made, 1)
            high(2, 0)
            act.wait_ge(beta_made, 2)

            def around(n, slot):
                wrap(n + 4, slot)
                evacuate(n, slot)
                high(n + 3, 1 - slot)

            for n in range(2):
                around(n, n)
            with act.Fori(1, NB // 2 - 2) as i:
                for c in range(2):
                    around(2 * i + c, c)
            evacuate(NB - 4, 0)
            high(NB - 1, 1)
            evacuate(NB - 3, 1)
            evacuate(NB - 2, 0, [0])
            bias(NB - 2, 0, 1)
            act.wait_ge(mix_done, 2 * NB - 2)
            place(0, 1, 0, yflat(0))
            place(0, 1, BANK, yflat(1)).then_inc(z_made, 1)
            evacuate(NB - 1, 1, [0])
            bias(NB - 1, 1, 1)
            for h in range(2):
                act.wait_ge(mix_done, 2 * NB + h)
                place(1, 1, BANK * h, yflat(2 + h)).then_inc(z_made, 1)

        @block.vector
        def _(dve):
            def columns(n, slot, r):
                if isinstance(n, int) and n < 1:
                    dve.wait_ge(wrapped_0, r + 1)
                elif r == 0:
                    dve.wait_ge(wrapped, n)
                    dve.wait_ge(turned, n)
                nc.vector.transpose(
                    xcol[:, :, :, :, r].rearrange("q b p c h -> q (b p) c h"),
                    xin[slot][:, r, 0:L].rearrange("q (b j p) -> q b p j", j=32, p=PH)).then_inc(cols_made, 1)

            def phases(n, slot):
                dve.wait_ge(cols_made, 2 * n + 2)
                if not (isinstance(n, int) and n < 2):
                    dve.wait_ge(lo_made, 2 * n - 2)
                nc.vector.transpose(
                    xph[slot][:, :, :, 0:NJ].rearrange("q s g (b j) -> q b (s g) j", j=32),
                    xcol[:].rearrange("q b p c r h -> q b (r h) (p c)")).then_inc(turned, 1)

            def edges(n, slot):
                v = xph[slot][:].bitcast(I32).rearrange("q s g j -> q j (s g)")
                dve.wait_ge(turned, n + 1)
                nc.vector.tensor_tensor(v[:, NJ::-NJ], v[:, 0:1].broadcast_to([P, 2, S * G]),
                                        ebits[:].unsqueeze(2).broadcast_to([P, 2, S * G]),
                                        ALU.bitwise_and).then_inc(edged, 1)

            def y_columns(n, g):
                dve.wait_ge(conv_done, 4 * n + g + 1)
                if g == 0 and not (isinstance(n, int) and n < 1):
                    dve.wait_ge(ynat_made, n)
                nc.vector.transpose(ycol[:, :, :, :, g].rearrange("q b c s -> q s b c"),
                                    yps[g][:].rearrange("q s (b j) -> q s b j", j=32)).then_inc(ycol_made, 1)

            def y_natural(n, slot):
                dve.wait_ge(ycol_made, 4 * n + 4)
                if not (isinstance(n, int) and n < 2):
                    dve.wait_ge(mix_done, 2 * n - 2)
                nc.vector.transpose(ynat[slot].rearrange("q r c -> q (r c)"),
                                    ycol[:].rearrange("q b c s g -> q (b c s g)")).then_inc(ynat_made, 1)

            def ahead(n, slot):
                for r in range(PR):
                    columns(n, slot, r)
                phases(n, slot)
                edges(n, slot)

            dve.wait_ge(e_in, 16)
            ahead(0, 0)
            dve.wait_ge(w_in, 16)
            nc.vector.tensor_tensor(wsum, wsum, residual.unsqueeze(2).broadcast_to([P, 2, G, P]),
                                    ALU.add).then_inc(w_sum, 1)
            dve.wait_ge(mm, 3)
            nc.vector.tensor_reduce(negmax[:], sps[:, 2 * NS:2 * NS + KE], AX.X, ALU.max, negate=True).then_inc(soft, 1)
            dve.wait_ge(w_hi, 1)
            nc.vector.tensor_tensor(wlo[:], wsum, whi[:].bitcast(F32), ALU.subtract).then_inc(w_lo, 1)
            dve.wait_ge(act_mlp, 3)
            nc.vector.reciprocal(erec[:], esum[:]).then_inc(soft, 1)
            nc.vector.tensor_copy(att[:, :, 2 * KE], parity[:, 0:1].broadcast_to([P, AO])).then_inc(soft, 1)
            dve.wait_ge(soft, 2)
            for k in range(2):
                nc.vector.tensor_scalar(att[:, :, KE * k:KE * k + KE], expv[:].unsqueeze(1).broadcast_to([P, AO, KE]),
                                        erec[:], parity[:, k:k + 1], ALU.mult, ALU.mult).then_inc(soft, 1)
            for r in range(PR):
                columns(1, 1, r)
            dve.wait_ge(mm, 4)
            nc.vector.tensor_tensor(attt[:], sps[0:AO * EX, 3 * NS:3 * NS + NP].unsqueeze(1).broadcast_to([AO * EX, AO, NP]),
                                    turn[0:AO * EX].unsqueeze(2).broadcast_to([AO * EX, AO, NP]), ALU.mult).then_inc(soft, 1)
            phases(1, 1)
            edges(1, 1)

            def step(n, slot, more=True):
                if more:
                    columns(n + 2, slot, 0)
                y_columns(n, 0)
                if more:
                    columns(n + 2, slot, 1)
                for g in range(1, G):
                    y_columns(n, g)
                if more:
                    phases(n + 2, slot)
                y_natural(n, slot)
                if more:
                    edges(n + 2, slot)

            for n in range(2):
                step(n, n)
            with dve.Fori(1, NB // 2 - 1) as i:
                for c in range(2):
                    step(2 * i + c, c)
            for n in range(NB - 2, NB):
                step(n, n % 2, more=False)

        @block.tensor
        def _(pe):
            def aggregate(a):
                if a >= 2:
                    pe.wait_ge(agg_out, a - 1)
                n = min(AO, C + 1 - AO * a)
                nc.tensor.matmul(zps[:, BANK * (a % 2):BANK * (a % 2) + NP * n].rearrange("p (o b) -> p o b", o=n),
                                 mixw[:, a], attt[:, 0:n], start=True, stop=True).then_inc(agg_mm, 1)

            def conv(n, slot, g):
                if g % 2 == 0:
                    pe.wait_ge(hi_made, 2 * n + g // 2 + 1)
                if not (isinstance(n, int) and n < 1):
                    pe.wait_ge(ycol_made, 4 * n - 3 + g)
                for i, (w, v) in enumerate([(whi, xhi), (wlo, xhi), (whi, xlo)]):
                    if i == 1 and isinstance(n, int) and n + g < 1:
                        pe.wait_ge(w_lo, 1)
                    if i == 2 and g % 2 == 0:
                        pe.wait_ge(lo_made, 2 * n + g // 2 + 1)
                    for b in range(2):
                        last = nc.tensor.matmul(yps[g][:].rearrange("p s (r j) -> p s r j", r=PR), w[:, b, g],
                                                v[slot][:, :, g, b:b + NJ].rearrange("p (r s) j -> p s r j", r=PR),
                                                start=i + b == 0, stop=i == 2 and b == 1)
                last.then_inc(conv_done, 1)

            def mix(n, slot, r, banks=(), each=False):
                if r == 0:
                    pe.wait_ge(ynat_made, n + 1)
                pe.wait_ge(mixv_made, 2 * n + r + 1)
                if isinstance(n, int) and n + r < 1:
                    pe.wait_ge(beta_made, 2)
                else:
                    pe.wait_ge(gam_made, 2 * n + r)
                nc.tensor.matmul(gps[:, 2 * slot + r:2 * slot + r + 1], mixv[slot][:, r], beta[:, 0, bass.ds(2 * n + r, 1)],
                                 start=True, stop=True).then_inc(gam_mm, 1)
                if isinstance(n, int) and n == NB - 1 and r == 0:
                    pe.wait_ge(z_made, 2 * n - 1)
                elif not banks and not (isinstance(n, int) and n < 1 and r == 0):
                    pe.wait_ge(z_made, 2 * n + r)
                for h in range(2):
                    last = nc.tensor.matmul(yflat(banks[h]) if banks else zps[:, BANK * h:BANK * h + BANK],
                                            mixv[slot][:, r], ynat[slot][:, r, BANK * h:BANK * h + BANK],
                                            start=True, stop=True)
                    if each or h == 1:
                        last.then_inc(mix_done, 1)

            def both(n, slot):
                conv(n, slot, 2)
                conv(n, slot, 3)
                for r in range(PR):
                    mix(n - 1, 1 - slot, r)
                    conv(n + 1, 1 - slot, r)

            pe.wait_ge(mlp_in, 16)
            nc.tensor.matmul(sps[:, 0:NS], w0s, condt, start=True, stop=True).then_inc(mm, 1)
            pe.wait_ge(act_mlp, 1)
            nc.tensor.matmul(sps[:, NS:2 * NS], w1s, h1[:], start=True, stop=True).then_inc(mm, 1)
            pe.wait_ge(act_mlp, 2)
            nc.tensor.matmul(sps[:, 2 * NS:2 * NS + KE], h2[:], w2s, start=True, stop=False)
            nc.tensor.matmul(sps[:, 2 * NS:2 * NS + KE], ones[0:1], b2s[0:1], start=False, stop=True).then_inc(mm, 1)
            pe.wait_ge(cw_in, 16)
            for k in range(2):
                last = nc.tensor.matmul(gps[:, NP:2 * NP], cws[:, k], condt[:, k::2], start=k == 0, stop=k == 1)
            last.then_inc(beta_mm, 1)
            pe.wait_ge(w_hi, 1)
            conv(0, 0, 0)
            pe.wait_ge(soft, 5)
            nc.tensor.matmul(sps[0:AO * EX, 3 * NS:3 * NS + NP], att[:].rearrange("p o e -> p (o e)"), pairs,
                             start=True, stop=True).then_inc(mm, 1)
            for g in range(1, G):
                conv(0, 0, g)
            pe.wait_ge(soft, 6)
            pe.wait_ge(mix_in, 16)
            for a in range(AGG):
                if a in (3, 5, 7):
                    conv(1, 1, (a - 3) // 2)
                aggregate(a)
            conv(1, 1, 3)
            for r in range(PR):
                mix(0, 0, r)
                conv(2, 0, r)
            with pe.Fori(1, NB // 2 - 1) as i:
                both(2 * i, 0)
                both(2 * i + 1, 1)
            both(NB - 2, 0)
            conv(NB - 1, 1, 2)
            conv(NB - 1, 1, 3)
            mix(NB - 2, 0, 0)
            pe.wait_ge(ycol_made, 4 * NB - 2)
            mix(NB - 2, 0, 1, banks=(0, 1))
            mix(NB - 1, 1, 0)
            mix(NB - 1, 1, 1, banks=(2, 3), each=True)


def constants():
    k, r = np.arange(P) // 32, np.arange(P) % 32
    phase, cc = r // CC, r % CC
    alike = (k[:, None] == k) & (cc[:, None] == cc)
    gap = phase[:, None] - phase
    residual = np.stack([alike & (gap == TAPS // 2), alike & (gap + PH == TAPS // 2)], 1)
    s = np.arange(P) // G % 2
    smask = s[:, None] == np.arange(2)
    parity = np.arange(NS)[:, None] % 2 == np.arange(2)
    pairs = np.arange(NS)[:, None] // 2 == np.arange(NP)
    turn = np.arange(P)[:, None] // EX == np.arange(AO)
    ebits = -np.stack([phase < PAD, phase >= PAD], 1).astype(np.int32)
    return residual.astype(np.float32), smask, parity, pairs, turn, ebits


def rows(v):
    v = v.reshape(-1, G, CG).transpose(0, 2, 1)[:, :, None, :]
    return np.broadcast_to(v, (v.shape[0], CG, 2, G)).reshape(-1, P)


def by_sample(v):
    s = np.arange(P) // G % 2
    return np.stack([np.where(s == k, v, np.zeros_like(v)) for k in range(2)])


def conv_places(w):
    w = w.reshape(G, KQ, CC, KQ, CC, TAPS).transpose(3, 4, 0, 1, 2, 5)
    at = np.zeros((KQ, PH, CC, 2, G, KQ, PH, CC), w.dtype)
    for b in range(2):
        for p in range(PH):
            for q in range(PH):
                if 0 <= p - q + PH * b < TAPS:
                    at[:, p, :, b, :, :, q, :] = w[..., p - q + PH * b]
    return at.reshape(P, 2 * G, P)


def kernel(**inputs):
    import concourse.bacc as bacc
    from concourse.bass_utils import run_bass_kernel_spmd

    a = {n: np.asarray(v) for n, v in inputs.items()}
    residual, smask, parity, pairs, turn, ebits = constants()
    out_c = a["L1_cond_weight"].reshape(KE, G, CG, C).transpose(0, 2, 1, 3).reshape(KE * C, C)
    mix_w = by_sample(rows(out_c).reshape(KE, C, P))
    bias_k = by_sample(rows(a["L1_cond_bias_k"]))[:, :, None]
    same = rows(np.eye(C, dtype=np.float32).reshape(G, CG, C).transpose(1, 0, 2).reshape(C, C))
    experts = np.concatenate([mix_w, bias_k], 2).reshape(2 * KE, C + 1, P)
    identity = np.concatenate([same, np.zeros((1, P), np.float32)])[None]
    mix_w = np.zeros((EX, AGG * AO, P), np.float32)
    mix_w[:, :C + 1] = np.concatenate([experts, identity])
    mix_w = mix_w.reshape(EX, AGG, AO, P).transpose(2, 0, 1, 3).reshape(AO * EX, AGG, P)
    mlp = np.zeros((P, MLP_COLS), np.float32)
    at = 0
    for name, v in {
            "condt": a["cond_128"].T, "w0": a["L1_cond_W0"], "w1": a["L1_cond_W1"], "w2": a["L1_cond_W2"],
            "b0": a["L1_cond_b0"][:, None], "b1": a["L1_cond_b1"][:, None], "fside": rows(a["fside_S_0"]).T,
            "smask": smask, "parity": parity, "pairs": pairs, "turn": turn, "ones": np.ones((1, P)), "b2": a["L1_cond_b2"][None]}.items():
        mlp[:len(v), at:at + MLP_PARTS[name]] = v
        at += MLP_PARTS[name]
    arrays = {
        "x": a["x"], "conv_w": np.concatenate([conv_places(a["L0_cond_weight"]), residual], 1), "mlp": mlp,
        "cond_w": by_sample(rows(a["L0_cond_c_weight"].T)).transpose(1, 0, 2),
        "mix_w": mix_w, "ebits": ebits,
    }
    arrays = {f"in_{n}": np.ascontiguousarray(v) for n, v in arrays.items()}
    nc = bacc.Bacc("TRN2", target_bir_lowering=False, num_devices=1)
    args = [nc.dram_tensor(n, v.shape, mybir.dt.from_np(v.dtype), kind="ExternalInput").ap() for n, v in arrays.items()]
    args.append(nc.dram_tensor("out", (NS, C, L), F32, kind="ExternalOutput").ap())
    build(nc, *args)
    r = run_bass_kernel_spmd(nc, [arrays], core_ids=[0])
    return r.results[0]["out"]
```
